# Optimizing a Trainium2 kernel written in Bass

```python
import numpy as np
import jax
import jax.numpy as jnp

def _softmax(x, axis=-1):
    return jax.nn.softmax(x, axis=axis)

def _gelu(x):
    return jax.nn.gelu(x, approximate=True)

def _silu(x):
    return jax.nn.silu(x)

def _sigmoid(x):
    return jax.nn.sigmoid(x)

def _layernorm(x, axis=-1, eps=1e-05):
    m = jnp.mean(x, axis=axis, keepdims=True)
    v = jnp.var(x, axis=axis, keepdims=True)
    return (x - m) / jnp.sqrt(v + eps)

def _scatter_add(tgt, idx, src, axis=0):
    return tgt.at[idx].add(src)

def _segment_sum(src, seg, n):
    return jax.ops.segment_sum(src, seg, n)
kernel_name = 'mk_gnn_resnorm_d4_gnn_r32_5a216a'

def setup_inputs(seed: int=0):
    np.random.seed(seed)
    _w = jnp.asarray

    def _rec_inputs():
        import jax
        import jax.numpy as jnp
        _gk = jax.random.key(seed)
        x = -0.000202 + 1 * jax.random.normal(jax.random.fold_in(_gk, 1), (50000, 128), jnp.float32)
        src = jax.random.randint(jax.random.fold_in(_gk, 2), (50000,), 0, 50000, jnp.int32)
        dst = jnp.minimum((50000 * jax.random.uniform(jax.random.fold_in(_gk, 3), (50000,)) ** 2.0).astype(jnp.int32), 49999)
        _o = jnp.argsort(dst, stable=True)
        src = src[_o]
        dst = dst[_o]
        edge_attr_8 = 0.000398945 + 1.00003 * jax.random.normal(jax.random.fold_in(_gk, 11), (50000, 8), jnp.float32)
        edge_weight = jax.random.uniform(jax.random.fold_in(_gk, 13), (50000,), jnp.float32, 0.0, 0.999998)
        return (x, src, dst, edge_attr_8, edge_weight)
    x, src, dst, edge_attr_8, edge_weight = _rec_inputs()

    def _L0_gnn_setup():
        import jax, jax.numpy as jnp
        import numpy as np
        N, C, E = (50000, 128, 18750)
        EPS = 1e-05
        SLOPE = 0.2

        def layer_norm(h, g, b):
            m = jnp.mean(h, axis=-1, keepdims=True)
            v = jnp.mean((h - m) ** 2, axis=-1, keepdims=True)
            return (h - m) * jax.lax.rsqrt(v + EPS) * g + b
        key = jax.random.key(seed)
        ks = jax.random.split(key, 12)
        s1 = 1.0 / np.sqrt(2 * C)
        s2 = 1.0 / np.sqrt(C)
        return {'x': jax.random.normal(ks[0], (N, C), dtype=jnp.float32), 'edge_index': jax.random.randint(ks[1], (2, E), 0, N, dtype=jnp.int64), 'edge_attr': jax.random.uniform(ks[2], (E,), dtype=jnp.float32), 'w1': jax.random.uniform(ks[3], (2 * C, C), jnp.float32, -s1, s1), 'b1': jax.random.uniform(ks[4], (C,), jnp.float32, -s1, s1), 'g1': jnp.ones((C,), jnp.float32), 'be1': jnp.zeros((C,), jnp.float32), 'w2': jax.random.uniform(ks[5], (C, C), jnp.float32, -s2, s2), 'b2': jax.random.uniform(ks[6], (C,), jnp.float32, -s2, s2), 'g2': jnp.ones((C,), jnp.float32), 'be2': jnp.zeros((C,), jnp.float32)}
    _L0_gnn_all = _L0_gnn_setup()
    _L0_gnn_in = {k: v for k, v in _L0_gnn_all.items() if k in ('w1', 'b1', 'g1', 'be1', 'w2', 'b2', 'g2', 'be2')}
    del _L0_gnn_all

    def _L1_gnn_setup():
        import jax, jax.numpy as jnp
        import numpy as np
        N_NODES = 10000
        N_EDGES = 20000
        D_IN = 128
        D_H = 128

        def _sage_conv(h, src, dst, n_nodes, W_self, W_neigh, b):
            msg = h[src]
            agg = jax.ops.segment_sum(msg, dst, num_segments=n_nodes)
            deg = jax.ops.segment_sum(jnp.ones_like(dst, dtype=h.dtype), dst, num_segments=n_nodes)
            mean = agg / jnp.maximum(deg, 1.0)[:, None]
            return h @ W_self + mean @ W_neigh + b
        key = jax.random.key(seed)
        ks = jax.random.split(key, 8)
        x = jax.random.normal(ks[0], (N_NODES, D_IN), dtype=jnp.float32)
        edge_index = jax.random.randint(ks[1], (2, N_EDGES), 0, N_NODES, dtype=jnp.int64)
        s1 = 1.0 / np.sqrt(D_IN)
        s2 = 1.0 / np.sqrt(D_H)
        W_self1 = jax.random.normal(ks[2], (D_IN, D_H), dtype=jnp.float32) * s1
        W_neigh1 = jax.random.normal(ks[3], (D_IN, D_H), dtype=jnp.float32) * s1
        b1 = jnp.zeros((D_H,), dtype=jnp.float32)
        W_self2 = jax.random.normal(ks[4], (D_H, D_H), dtype=jnp.float32) * s2
        W_neigh2 = jax.random.normal(ks[5], (D_H, D_H), dtype=jnp.float32) * s2
        b2 = jnp.zeros((D_H,), dtype=jnp.float32)
        return {'x': x, 'edge_index': edge_index, 'W_self1': W_self1, 'W_neigh1': W_neigh1, 'b1': b1, 'W_self2': W_self2, 'W_neigh2': W_neigh2, 'b2': b2}
    _L1_gnn_all = _L1_gnn_setup()
    _L1_gnn_in = {k: v for k, v in _L1_gnn_all.items() if k in ('W_self1', 'W_neigh1', 'b1', 'W_self2', 'W_neigh2', 'b2')}
    del _L1_gnn_all

    def _L2_gnn_setup():
        import jax, jax.numpy as jnp
        import numpy as np
        N_NODES = 3125
        N_EDGES = 50000
        IN_DIM = 128
        HID_DIM = 128

        def _gcn_norm(edge_index, num_nodes):
            loops = jnp.arange(num_nodes, dtype=edge_index.dtype)
            src = jnp.concatenate([edge_index[0], loops])
            dst = jnp.concatenate([edge_index[1], loops])
            deg = jax.ops.segment_sum(jnp.ones_like(dst, dtype=jnp.float32), dst, num_segments=num_nodes)
            dinv = jnp.where(deg > 0, jax.lax.rsqrt(deg), 0.0)
            norm = dinv[src] * dinv[dst]
            return (src, dst, norm)

        def _gcn_conv(x, W, b, src, dst, norm, num_nodes):
            h = x @ W
            msg = h[src] * norm[:, None]
            out = jax.ops.segment_sum(msg, dst, num_segments=num_nodes)
            return out + b
        key = jax.random.key(seed)
        k_x, k_e, k_w1, k_w2 = jax.random.split(key, 4)
        x = jax.random.normal(k_x, (N_NODES, IN_DIM), dtype=jnp.float32)
        edge_index = jax.random.randint(k_e, (2, N_EDGES), 0, N_NODES, dtype=jnp.int64)
        s1 = 1.0 / np.sqrt(IN_DIM)
        s2 = 1.0 / np.sqrt(HID_DIM)
        W1 = jax.random.uniform(k_w1, (IN_DIM, HID_DIM), jnp.float32, -s1, s1)
        b1 = jnp.zeros((HID_DIM,), jnp.float32)
        W2 = jax.random.uniform(k_w2, (HID_DIM, HID_DIM), jnp.float32, -s2, s2)
        b2 = jnp.zeros((HID_DIM,), jnp.float32)
        return {'x': x, 'edge_index': edge_index, 'W1': W1, 'b1': b1, 'W2': W2, 'b2': b2}
    _L2_gnn_all = _L2_gnn_setup()
    _L2_gnn_in = {k: v for k, v in _L2_gnn_all.items() if k in ('W1', 'b1', 'W2', 'b2')}
    del _L2_gnn_all

    def _L3_gnn_setup():
        import jax, jax.numpy as jnp
        import numpy as np
        N = 50000
        E = 25000
        F = 128
        H = 8
        D = F // H
        key = jax.random.key(seed)
        ks = jax.random.split(key, 12)
        s = 0.02
        return {'node_features': jax.random.normal(ks[0], (N, F), dtype=jnp.float32), 'edge_index': jax.random.randint(ks[1], (2, E), 0, N, dtype=jnp.int32), 'attention_mask': jax.random.normal(ks[2], (E, H), dtype=jnp.float32), 'Wq': jax.random.normal(ks[3], (F, F), dtype=jnp.float32) * s, 'bq': jnp.zeros((F,), dtype=jnp.float32), 'Wk': jax.random.normal(ks[4], (F, F), dtype=jnp.float32) * s, 'bk': jnp.zeros((F,), dtype=jnp.float32), 'Wv': jax.random.normal(ks[5], (F, F), dtype=jnp.float32) * s, 'bv': jnp.zeros((F,), dtype=jnp.float32), 'Wo': jax.random.normal(ks[6], (F, F), dtype=jnp.float32) * s, 'bo': jnp.zeros((F,), dtype=jnp.float32)}
    _L3_gnn_all = _L3_gnn_setup()
    _L3_gnn_in = {k: v for k, v in _L3_gnn_all.items() if k in ('Wq', 'bq', 'Wk', 'bk', 'Wv', 'bv', 'Wo', 'bo')}
    del _L3_gnn_all
    return {'x': x, 'src': src, 'dst': dst, 'edge_attr_8': edge_attr_8, 'edge_weight': edge_weight, 'L0_gnn_w1': _L0_gnn_in['w1'], 'L0_gnn_b1': _L0_gnn_in['b1'], 'L0_gnn_g1': _L0_gnn_in['g1'], 'L0_gnn_be1': _L0_gnn_in['be1'], 'L0_gnn_w2': _L0_gnn_in['w2'], 'L0_gnn_b2': _L0_gnn_in['b2'], 'L0_gnn_g2': _L0_gnn_in['g2'], 'L0_gnn_be2': _L0_gnn_in['be2'], 'L1_gnn_W_self1': _L1_gnn_in['W_self1'], 'L1_gnn_W_neigh1': _L1_gnn_in['W_neigh1'], 'L1_gnn_b1': _L1_gnn_in['b1'], 'L1_gnn_W_self2': _L1_gnn_in['W_self2'], 'L1_gnn_W_neigh2': _L1_gnn_in['W_neigh2'], 'L1_gnn_b2': _L1_gnn_in['b2'], 'L2_gnn_W1': _L2_gnn_in['W1'], 'L2_gnn_b1': _L2_gnn_in['b1'], 'L2_gnn_W2': _L2_gnn_in['W2'], 'L2_gnn_b2': _L2_gnn_in['b2'], 'L3_gnn_Wq': _L3_gnn_in['Wq'], 'L3_gnn_bq': _L3_gnn_in['bq'], 'L3_gnn_Wk': _L3_gnn_in['Wk'], 'L3_gnn_bk': _L3_gnn_in['bk'], 'L3_gnn_Wv': _L3_gnn_in['Wv'], 'L3_gnn_bv': _L3_gnn_in['bv'], 'L3_gnn_Wo': _L3_gnn_in['Wo'], 'L3_gnn_bo': _L3_gnn_in['bo']}

def reference(x, src, dst, edge_attr_8, edge_weight, L0_gnn_w1, L0_gnn_b1, L0_gnn_g1, L0_gnn_be1, L0_gnn_w2, L0_gnn_b2, L0_gnn_g2, L0_gnn_be2, L1_gnn_W_self1, L1_gnn_W_neigh1, L1_gnn_b1, L1_gnn_W_self2, L1_gnn_W_neigh2, L1_gnn_b2, L2_gnn_W1, L2_gnn_b1, L2_gnn_W2, L2_gnn_b2, L3_gnn_Wq, L3_gnn_bq, L3_gnn_Wk, L3_gnn_bk, L3_gnn_Wv, L3_gnn_bv, L3_gnn_Wo, L3_gnn_bo):
    import jax
    import jax.numpy as jnp

    def _L0_gnn_ref(x, edge_index, edge_attr, w1, b1, g1, be1, w2, b2, g2, be2):
        import jax, jax.numpy as jnp
        import numpy as np
        N, C, E = (50000, 128, 18750)
        EPS = 1e-05
        SLOPE = 0.2

        def layer_norm(h, g, b):
            m = jnp.mean(h, axis=-1, keepdims=True)
            v = jnp.mean((h - m) ** 2, axis=-1, keepdims=True)
            return (h - m) * jax.lax.rsqrt(v + EPS) * g + b
        source, target = (edge_index[0], edge_index[1])
        ef = jnp.concatenate([x[source], x[target]], axis=1)
        h = jax.nn.leaky_relu(layer_norm(ef @ w1 + b1, g1, be1), SLOPE)
        h = jax.nn.leaky_relu(layer_norm(h @ w2 + b2, g2, be2), SLOPE)
        h = h * edge_attr[:, None]
        out = jax.ops.segment_sum(h, target, num_segments=N)
        return out

    def _L1_gnn_ref(x, edge_index, W_self1, W_neigh1, b1, W_self2, W_neigh2, b2):
        import jax, jax.numpy as jnp
        import numpy as np
        N_NODES = 10000
        N_EDGES = 20000
        D_IN = 128
        D_H = 128

        def _sage_conv(h, src, dst, n_nodes, W_self, W_neigh, b):
            msg = h[src]
            agg = jax.ops.segment_sum(msg, dst, num_segments=n_nodes)
            deg = jax.ops.segment_sum(jnp.ones_like(dst, dtype=h.dtype), dst, num_segments=n_nodes)
            mean = agg / jnp.maximum(deg, 1.0)[:, None]
            return h @ W_self + mean @ W_neigh + b
        n_nodes = x.shape[0]
        src, dst = (edge_index[0], edge_index[1])
        h = _sage_conv(x, src, dst, n_nodes, W_self1, W_neigh1, b1)
        h = jax.nn.relu(h)
        h = _sage_conv(h, src, dst, n_nodes, W_self2, W_neigh2, b2)
        return h

    def _L2_gnn_ref(x, edge_index, W1, b1, W2, b2):
        import jax, jax.numpy as jnp
        import numpy as np
        N_NODES = 3125
        N_EDGES = 50000
        IN_DIM = 128
        HID_DIM = 128

        def _gcn_norm(edge_index, num_nodes):
            loops = jnp.arange(num_nodes, dtype=edge_index.dtype)
            src = jnp.concatenate([edge_index[0], loops])
            dst = jnp.concatenate([edge_index[1], loops])
            deg = jax.ops.segment_sum(jnp.ones_like(dst, dtype=jnp.float32), dst, num_segments=num_nodes)
            dinv = jnp.where(deg > 0, jax.lax.rsqrt(deg), 0.0)
            norm = dinv[src] * dinv[dst]
            return (src, dst, norm)

        def _gcn_conv(x, W, b, src, dst, norm, num_nodes):
            h = x @ W
            msg = h[src] * norm[:, None]
            out = jax.ops.segment_sum(msg, dst, num_segments=num_nodes)
            return out + b
        n = x.shape[0]
        src, dst, norm = _gcn_norm(edge_index, n)
        h = _gcn_conv(x, W1, b1, src, dst, norm, n)
        h = jax.nn.relu(h)
        return _gcn_conv(h, W2, b2, src, dst, norm, n)

    def _L3_gnn_ref(node_features, edge_index, attention_mask, Wq, bq, Wk, bk, Wv, bv, Wo, bo):
        import jax, jax.numpy as jnp
        import numpy as np
        N = 50000
        E = 25000
        F = 128
        H = 8
        D = F // H
        src, dest = (edge_index[0], edge_index[1])
        q = (node_features @ Wq.T + bq).reshape(N, H, D)
        k = (node_features @ Wk.T + bk).reshape(N, H, D)
        v = (node_features @ Wv.T + bv).reshape(N, H, D)
        scores = jnp.sum(q[src] * k[dest], axis=-1) / jnp.sqrt(jnp.float32(D))
        scores = scores + attention_mask
        seg_max = jax.ops.segment_max(scores, src, num_segments=N)
        ex = jnp.exp(scores - seg_max[src])
        seg_sum = jax.ops.segment_sum(ex, src, num_segments=N)
        weights = ex / seg_sum[src]
        weighted = v[src] * weights[:, :, None]
        out = jax.ops.segment_sum(weighted, dest, num_segments=N)
        out = out.reshape(N, F)
        return out @ Wo.T + bo
    edge_index = jnp.stack([src, dst])
    x = _layernorm(x + _L0_gnn_ref(x, edge_index, edge_weight, L0_gnn_w1, L0_gnn_b1, L0_gnn_g1, L0_gnn_be1, L0_gnn_w2, L0_gnn_b2, L0_gnn_g2, L0_gnn_be2), axis=-1)
    x = _layernorm(x + _L1_gnn_ref(x, edge_index, L1_gnn_W_self1, L1_gnn_W_neigh1, L1_gnn_b1, L1_gnn_W_self2, L1_gnn_W_neigh2, L1_gnn_b2), axis=-1)
    x = _layernorm(x + _L2_gnn_ref(x, edge_index, L2_gnn_W1, L2_gnn_b1, L2_gnn_W2, L2_gnn_b2), axis=-1)
    x = _layernorm(x + _L3_gnn_ref(x, edge_index, edge_attr_8, L3_gnn_Wq, L3_gnn_bq, L3_gnn_Wk, L3_gnn_bk, L3_gnn_Wv, L3_gnn_bv, L3_gnn_Wo, L3_gnn_bo), axis=-1)
    return x

_drawn_inputs = setup_inputs


def setup_inputs(seed=0):
    import zlib

    import numpy as np

    out = dict(_drawn_inputs(seed))
    spreads = {'L0_gnn_g1': (1.0, 0.2),
     'L0_gnn_be1': (0.0, 0.274),
     'L0_gnn_g2': (1.0, 0.2),
     'L0_gnn_be2': (0.0, 0.1),
     'L1_gnn_b1': (0.0, 0.1),
     'L1_gnn_b2': (0.0, 0.1),
     'L2_gnn_b1': (0.0, 0.1),
     'L2_gnn_b2': (0.0, 0.1),
     'L3_gnn_bq': (0.0, 2.0),
     'L3_gnn_bk': (0.0, 2.0),
     'L3_gnn_bv': (0.0, 0.374),
     'L3_gnn_bo': (0.0, 0.1)}
    factors = {'edge_attr_8': 21.625, 'L3_gnn_Wq': 24.095, 'L3_gnn_Wk': 23.371}
    for name, (base, spread) in spreads.items():
        noise = np.random.default_rng([zlib.crc32(name.encode()), seed]).standard_normal(out[name].shape)
        drawn = base * np.exp(spread * noise) if base else spread * noise
        out[name] = jnp.asarray(drawn.astype(out[name].dtype))
    for name, factor in factors.items():
        out[name] = (out[name] * factor).astype(out[name].dtype)
    return out
```

```python
import concourse.bass as bass
from concourse import mybir
from contextlib import ExitStack

F32 = mybir.dt.float32
BF16 = mybir.dt.bfloat16
I32 = mybir.dt.int32
ALU = mybir.AluOpType
ACT = mybir.ActivationFunctionType
AX_X = mybir.AxisListType.X
ds = bass.ds

P = 128
C = 128
N = 50000
E = 50000
NT = 392
ET = 392
NP = NT * P
STEPS = NT + ET
Q = 4
TQ = 98
PAD_DST = 60000
PAD_SRC = NP - 1
RING = 8
EPS = 1e-5
SLOPE = 0.2
HEADS = 8
DH = C // HEADS


class Chain:

    def __init__(self, eng, sem, per_iteration=0):
        self.eng, self.sem, self.per, self.base, self.n = eng, sem, per_iteration, 0, 0

    def at(self, i):
        assert self.n in (0, self.per)
        self.base, self.n = i * self.per, 0

    def link(self, ins):
        self.n += 1
        ins.then_inc(self.sem, 1)
        self.eng.wait_ge(self.sem, self.base + self.n)


class Core:
    pass


def phase(nc, name, sem_names):
    return {s: nc.alloc_semaphore(f"{name}_{s}") for s in sem_names}


def end_phase(nc, sems):
    nc.clear_and_free_semaphores(list(sems.values()))
    nc.all_engine_barrier()


def setup(nc, k, ins):
    sm = phase(nc, "setup", ["loaded", "iota", "dve", "pe_ready", "pe"])
    with ExitStack() as ctx:
        def sb(name, shape, dt=F32):
            return ctx.enter_context(nc.sbuf_tensor(name, shape, dt))

        def pb(name, shape):
            return ctx.enter_context(nc.psum_tensor(name, shape, F32))

        iota_i = sb("iota_i", [P, STEPS], I32)
        pid_i = sb("pid_i", [P, 1], I32)
        dst_f = sb("dst_f", [P, ET])
        dst_min = sb("dst_min", [P, ET])
        dT = sb("dT", [TQ, 4, P])
        bound = sb("bound", [P, NT])
        tile_ends = sb("tile_ends", [TQ, 4, NT])
        h_b = sb("h_b", [P, NT])
        hcol = sb("hcol", [TQ, 4])
        mcol = sb("mcol", [TQ, 4])
        past = sb("past", [TQ, 4, STEPS])
        left = sb("left", [TQ, 4, ET])
        ns = sb("ns", [P, STEPS])
        es = sb("es", [P, STEPS])
        es_i = sb("es_i", [1, STEPS], I32)
        tmp = sb("tmp_steps", [1, STEPS])
        pT = pb("pT", [P, 4, P])
        pH = pb("pH", [P, NT])
        pHT = pb("pHT", [P, 4, P])
        pN = [pb(f"pN{i}", [P, NT]) for i in range(2)]
        pL = pb("pL", [P, ET])

        with nc.Block() as block:
            @block.sync
            def _(sp):
                sp.dma_start(k.dst_i[:, :], ins["dst"]).then_inc(sm["loaded"], 16)
                sp.dma_start(k.src_i[:, :], ins["src"]).then_inc(sm["loaded"], 16)
                sp.dma_start(k.ew[:, :], ins["edge_weight"]).then_inc(sm["loaded"], 16)

            @block.gpsimd
            def _(pool):
                nc.gpsimd.iota(iota_i[:, :], pattern=[[1, STEPS]], base=0, channel_multiplier=0).then_inc(sm["iota"], 1)
                nc.gpsimd.iota(pid_i[:, :], pattern=[[0, 1]], base=0, channel_multiplier=1).then_inc(sm["iota"], 1)

            @block.vector
            def _(dve):
                v = nc.vector
                c = Chain(dve, sm["dve"])
                dve.wait_ge(sm["iota"], 2)
                c.link(v.tensor_copy(k.iota[:, :], iota_i[:, :]))
                c.link(v.tensor_copy(k.pid[:, :], pid_i[:, :]))
                c.link(v.tensor_scalar(k.ident[:, :], k.iota[:, 0:P], k.pid[:, 0:1], None, ALU.is_equal))
                c.link(v.memset(k.ones[:, :], 1.0))
                dve.wait_ge(sm["loaded"], 48)
                c.link(v.tensor_copy(dst_f[:, :], k.dst_i[:, :]))
                c.link(v.tensor_scalar(dst_min[:, :], dst_f[:, :], float(NP - 1), None, ALU.min))
                c.link(v.tensor_copy(k.dst_row[:, :], dst_min[:, :]))
                v.tensor_scalar(bound[:, :], k.iota[:, 0:NT], float(P), float(P), ALU.mult, ALU.add).then_inc(sm["pe_ready"], 1)
                dve.wait_ge(sm["pe"], 4)
                c.link(v.tensor_copy(dT[:, :, :], pT[0:TQ, :, :]))
                for q in range(4):
                    rows = TQ - (q == 3)
                    if q == 3:
                        c.link(v.memset(tile_ends[:, 3, :], 0.0))
                    c.link(v.tensor_scalar(tile_ends[0:rows, q, :], bound[0:rows, :], dT[0:rows, q, P - 1:P], None, ALU.is_gt))
                dve.sem_inc(sm["pe_ready"], 1)
                dve.wait_ge(sm["pe"], 5)
                c.link(v.tensor_copy(h_b[:, :], pH[:, :]))
                c.link(v.tensor_tensor(k.last_step[:, :], h_b[:, :], k.iota[:, 0:NT], ALU.add))
                c.link(v.tensor_copy(k.last_step_i[0:1, :], k.last_step[0:1, :]))
                dve.sem_inc(sm["pe_ready"], 1)
                dve.wait_ge(sm["pe"], 9)
                for q in range(4):
                    c.link(v.tensor_copy(hcol[:, q:q + 1], pHT[0:TQ, q, 0:1]))
                    c.link(v.tensor_scalar(mcol[:, q:q + 1], hcol[:, q:q + 1], k.pid[0:TQ, 0:1], float(TQ * q), ALU.add, ALU.add))
                    c.link(v.tensor_scalar(past[:, q, :], k.iota[0:TQ, :], mcol[:, q:q + 1], None, ALU.is_gt))
                    c.link(v.tensor_scalar(left[:, q, :], k.iota[0:TQ, 0:ET], hcol[:, q:q + 1], None, ALU.is_ge))
                dve.sem_inc(sm["pe_ready"], 1)
                dve.wait_ge(sm["pe"], 12)
                for j in range(2):
                    c.link(v.tensor_copy(ns[:, j * NT:(j + 1) * NT], pN[j][:, :]))
                c.link(v.scalar_tensor_tensor(tmp[0:1, 0:ET], k.iota[0:1, 0:ET], 1.0, pL[0:1, :], ALU.add, ALU.add))
                c.link(v.tensor_copy(k.left_step_i[0:1, :], tmp[0:1, 0:ET]))
                c.link(v.tensor_tensor(es[:, :], k.iota[:, :], ns[:, :], ALU.subtract))
                c.link(v.memset(k.keep[:, 0:1], 0.0))
                c.link(v.tensor_tensor(k.keep[:, 1:STEPS], ns[:, 1:STEPS], ns[:, 0:STEPS - 1], ALU.is_equal))
                c.link(v.tensor_copy(es_i[0:1, :], es[0:1, :]))
                c.link(v.tensor_scalar(k.slot_i[0:1, :], es_i[0:1, :], RING - 1, None, ALU.bitwise_and))
                c.link(v.tensor_scalar(tmp[0:1, :], es[0:1, :], 1.0, None, ALU.add))
                c.link(v.tensor_copy(k.arrive_i[0:1, :], tmp[0:1, :]))
                for q in range(4):
                    c.link(v.tensor_scalar(mcol[:, q:q + 1], k.pid[0:TQ, 0:1], float(TQ * q), None, ALU.add))
                    c.link(v.tensor_scalar(past[:, q, :], es[0:TQ, :], mcol[:, q:q + 1], None, ALU.is_equal))
                dve.sem_inc(sm["pe_ready"], 1)
                dve.wait_ge(sm["pe"], 14)
                for j in range(2):
                    part = slice(j * NT, (j + 1) * NT)
                    c.link(v.scalar_tensor_tensor(k.rel[:, part], ns[:, part], -float(P), pN[j][:, :], ALU.mult, ALU.add))

            @block.tensor
            def _(pe):
                t = nc.tensor
                pe.wait_ge(sm["pe_ready"], 1)
                for q in range(4):
                    t.transpose(pT[0:TQ, q, :], dst_f[:, q * TQ:(q + 1) * TQ], k.ident[:, :]).then_inc(sm["pe"], 1)
                pe.wait_ge(sm["pe_ready"], 2)
                for q in range(4):
                    last = t.matmul(pH[:, :], k.ones[0:TQ, :], tile_ends[:, q, :], start=q == 0, stop=q == 3)
                last.then_inc(sm["pe"], 1)
                pe.wait_ge(sm["pe_ready"], 3)
                for q in range(4):
                    t.transpose(pHT[0:TQ, q, :], h_b[:, q * TQ:(q + 1) * TQ], k.ident[:, :]).then_inc(sm["pe"], 1)
                pe.wait_ge(sm["pe_ready"], 4)
                for j in range(2):
                    for q in range(4):
                        last = t.matmul(pN[j][:, :], k.ones[0:TQ, :], past[:, q, j * NT:(j + 1) * NT], start=q == 0, stop=q == 3)
                    last.then_inc(sm["pe"], 1)
                for q in range(4):
                    last = t.matmul(pL[:, :], k.ones[0:TQ, :], left[:, q, :], start=q == 0, stop=q == 3)
                last.then_inc(sm["pe"], 1)
                pe.wait_ge(sm["pe_ready"], 5)
                for j in range(2):
                    for q in range(4):
                        last = t.matmul(pN[j][:, :], dT[:, q, :], past[:, q, j * NT:(j + 1) * NT], start=q == 0, stop=q == 3)
                    last.then_inc(sm["pe"], 1)
        end_phase(nc, sm)


def aggregate(nc, k, name, table, indices):
    GROUPS = STEPS // Q
    sm = phase(nc, name, [f"gathered{j}" for j in range(RING)] + ["rows", "slot_free", "arrived", "onehot", "summed", "acc", "written0", "written1", "written2", "written3"])
    gathered = [sm[f"gathered{j}"] for j in range(RING)]
    written = [sm[f"written{j}"] for j in range(4)]
    with ExitStack() as ctx:
        msgs = ctx.enter_context(nc.sbuf_tensor(name + "_msgs", [P, RING, C], F32))
        rows = ctx.enter_context(nc.sbuf_tensor(name + "_rows", [P, 2, RING], I32))
        onehot = ctx.enter_context(nc.sbuf_tensor(name + "_onehot", [P, 2, Q, P], F32))
        acc = ctx.enter_context(nc.sbuf_tensor(name + "_acc", [P, 4, Q, C], F32))
        sums = [ctx.enter_context(nc.psum_tensor(f"{name}_sums{j}", [P, Q, C], F32)) for j in range(4)]
        with nc.Block() as block:
            def load(pool, g, j, half, first):
                if not first:
                    pool.wait_ge(sm["summed"], pool.value_load(k.left_step_i[0:1, ds(g * RING + (j - RING), 1)], min_val=1, max_val=STEPS))
                    pool.sem_inc(sm["slot_free"], 1)
                if indices is None:
                    pool.dma_start(msgs[:, j, :], table[ds((g * RING + j) * P, P), :]).then_inc(gathered[j], 16)
                else:
                    pool.indirect_dma_start(msgs[:, j, :], None, table[:, :], bass.IndirectOffsetOnAxis(
                        ap=rows[:, half, j:j + 1], axis=0)).then_inc(gathered[j], 16)

            @block.gpsimd
            def _(pool):
                def loads(g, half, first):
                    if indices is not None:
                        nc.gpsimd.tensor_copy(rows[:, half, :], indices[:, ds(g * RING, RING)]).then_inc(sm["rows"], 1)
                        pool.wait_ge(sm["rows"], g + 1)
                        pool.sem_inc(sm["slot_free"], 1)
                    for j in range(RING):
                        load(pool, g, j, half, first)

                loads(0, 0, True)
                with pool.Fori(0, (ET // RING - 1) // 2) as i:
                    loads(i * 2 + 1, 1, False)
                    loads(i * 2 + 2, 0, False)

            @block.sync
            def _(sp):
                with sp.Fori(0, ET // RING) as g:
                    for j in range(RING):
                        sp.wait_ge(gathered[j], g * 16 + 16)
                        sp.sem_inc(sm["arrived"], 1)

            @block.vector
            def _(dve):
                def build(g, j, first):
                    if not first:
                        dve.wait_ge(sm["summed"], g * (4 * Q) + (j - 1) * Q)
                    nc.vector.tensor_tensor(
                        onehot[:, j % 2, :, :],
                        k.iota[:, 0:P].unsqueeze(1).to_broadcast([P, Q, P]),
                        k.rel[:, ds(g * (4 * Q) + j * Q, Q)].unsqueeze(2).to_broadcast([P, Q, P]),
                        ALU.is_equal).then_inc(sm["onehot"], 1)

                def gather_up(g, j, reused, first=False):
                    if reused:
                        dve.wait_ge(written[j], g * 16)
                    dve.wait_ge(sm["summed"], g * (4 * Q) + (j + 1) * Q)
                    for q in range(Q):
                        step = g * (4 * Q) + j * Q + q
                        before = acc[:, j, q - 1, :] if q else acc[:, (j - 1) % 4, Q - 1, :]
                        if first and q == 0:
                            nc.vector.tensor_copy(acc[:, j, q, :], sums[j][:, q, :]).then_inc(sm["acc"], 1)
                            continue
                        dve.wait_ge(sm["acc"], step)
                        nc.vector.scalar_tensor_tensor(acc[:, j, q, :], before, k.keep[:, ds(step, 1)], sums[j][:, q, :],
                                                       ALU.mult, ALU.add).then_inc(sm["acc"], 1)

                def round_of_four(g, number=None):
                    for j in range(4):
                        build(g, j, number == 0 and j < 2)
                        if j:
                            gather_up(g, j - 1, reused=number != 0, first=number == 0 and j == 1)
                        elif number != 0:
                            gather_up(g - 1, 3, reused=number != 1)

                round_of_four(0, 0)
                round_of_four(1, 1)
                with dve.Fori(2, GROUPS // 4) as g:
                    round_of_four(g)
                gather_up(GROUPS // 4 - 1, 3, reused=True)

            @block.tensor
            def _(pe):
                regs = [pe.alloc_register(f"{name}_slot{q}") for q in range(Q)]

                def steps(g, j, first):
                    if first:
                        at = j * Q
                    else:
                        at = g * (4 * Q) + j * Q
                    pe.reg_load(regs, k.slot_i[0:1, ds(at, Q)])
                    slots = [pe.snap(r, min_val=0, max_val=RING - 1) for r in regs]
                    pe.wait_ge(sm["arrived"], pe.value_load(k.arrive_i[0:1, ds(at + Q - 1, 1)], min_val=1, max_val=ET))
                    pe.wait_ge(sm["onehot"], (j + 1) if first else g * 4 + (j + 1))
                    if not first:
                        pe.wait_ge(sm["acc"], g * (4 * Q) + (j - 3) * Q)
                    for q in range(Q):
                        nc.tensor.matmul(sums[j][:, q, :], onehot[:, j % 2, q, :], msgs[:, slots[q], :],
                                         start=True, stop=True).then_inc(sm["summed"], 1)

                for j in range(4):
                    steps(0, j, True)
                with pe.Fori(1, GROUPS // 4) as g:
                    for j in range(4):
                        steps(g, j, False)

            @block.scalar
            def _(act):
                with act.Fori(0, GROUPS // 4) as g:
                    for j in range(4):
                        act.wait_ge(sm["acc"], g * (4 * Q) + (j + 1) * Q)
                        act.dma_start(k.partial[ds((g * 4 + j) * (Q * P), Q * P), :].rearrange("(q p) c -> p q c", p=P),
                                      acc[:, j, :, :]).then_inc(written[j], 16)
                for j in range(4):
                    act.wait_ge(written[j], 16 * (GROUPS // 4))
        end_phase(nc, sm)


AHEAD = 2
GROUPS = NT // Q


def rows_of(table, g):
    return table[ds(g * (Q * P), Q * P), :].rearrange("(q p) c -> p q c", p=P)


def count_and_rank(nc, k, ins):
    sm = phase(nc, "rank", ["c", "split", "hot", "hist", "used", "rooted", "moved", "pe_ready", "offset",
                            "row0", "row1", "turned", "copied", "looked", "ranked", "table", "looks_free"])
    with ExitStack() as ctx:
        def sb(name, shape, dt=F32):
            return ctx.enter_context(nc.sbuf_tensor(name, shape, dt))

        def pb(name, shape):
            return ctx.enter_context(nc.psum_tensor(name, shape, F32))

        part_i = sb("part_i", [P, ET], I32)
        lo = {"src": sb("src_lo", [P, ET]), "dst": sb("dst_lo", [P, ET])}
        hi = {"src": sb("src_hi", [P, ET]), "dst": sb("dst_hi", [P, ET])}
        src_f = sb("src_f", [P, ET])
        hot_lo = sb("hot_lo", [P, 2, 2, Q, P], BF16)
        hot_hi = sb("hot_hi", [P, 2, 2, Q, NT], BF16)
        zeros = sb("zeros", [P, NT], BF16)
        scan = sb("scan", [P, NT])
        one_row = sb("one_row", [P, NT])
        below = sb("below", [P, P])
        earlier = sb("earlier", [P, Q, Q * P])
        offset = sb("offset", [P, 1])
        run = sb("run", [P, NT])
        lo_f = sb("lo_f", [P, 2, Q, P])
        loT = sb("loT", [P, 2, Q, P])
        src_row = sb("src_row", [P, 2, Q * P], I32)
        base = sb("base", [P, 2, Q])
        rank = sb("rank", [P, 2, Q])
        rank_sink = sb("rank_sink", [P, Q, Q * P])
        look_sink = sb("look_sink", [P, Q, NT])
        pos_f = sb("pos_f", [P, ET])
        hist = {"dst": pb("hist_dst", [P, 512]), "src": pb("hist_src", [P, 512])}
        off = pb("off", [P, 512])
        turn = pb("turn", [P, Q, P])
        look = [pb(f"look{q}", [P, 512]) for q in range(Q)]

        with nc.Block() as block:
            @block.vector
            def _(dve):
                v = nc.vector
                c = Chain(dve, sm["c"])
                for name, idx in (("src", k.src_i), ("dst", k.dst_i)):
                    c.link(v.tensor_scalar(part_i[:, :], idx[:, :], P - 1, None, ALU.bitwise_and))
                    c.link(v.tensor_copy(lo[name][:, :], part_i[:, :]))
                    c.link(v.tensor_scalar(part_i[:, :], idx[:, :], 7, None, ALU.logical_shift_right))
                    c.link(v.tensor_copy(hi[name][:, :], part_i[:, :]))
                c.link(v.tensor_copy(src_f[:, :], k.src_i[:, :]))
                c.link(v.memset(zeros[:, :], 0.0))
                c.link(v.memset(one_row[:, :], 1.0))
                c.link(v.tensor_scalar(below[:, :], k.iota[:, 0:P], k.pid[:, 0:1], None, ALU.is_gt))
                for q in range(Q):
                    c.link(v.tensor_scalar(rank[:, 0, q:q + 1], k.pid[:, 0:1], float(P * q), None, ALU.add))
                    c.link(v.tensor_scalar(earlier[:, q, :], k.iota[:, 0:Q * P], rank[:, 0, q:q + 1], None, ALU.is_lt))
                dve.sem_inc(sm["split"], 1)
                dve.sem_inc(sm["used"], AHEAD)
                with dve.Fori(0, GROUPS // 2) as i:
                    for u in range(2):
                        dve.wait_ge(sm["used"], i * 2 + u + 1)
                        for w, name in enumerate(("dst", "src")):
                            for q in range(Q):
                                at = i * (2 * Q) + u * Q + q
                                v.tensor_scalar(hot_lo[:, u, w, q, :], k.iota[:, 0:P], lo[name][:, ds(at, 1)], None, ALU.is_equal)
                                last = v.tensor_scalar(hot_hi[:, u, w, q, :], k.iota[:, 0:NT], hi[name][:, ds(at, 1)], None, ALU.is_equal)
                        last.then_inc(sm["hot"], 1)
                dve.wait_ge(sm["hist"], 1)
                c.link(v.tensor_scalar(k.inv_deg[:, :], hist["dst"][:, 0:NT], 1.0, None, ALU.max))
                c.link(v.reciprocal(k.inv_deg[:, :], k.inv_deg[:, :]))
                c.link(v.tensor_scalar(k.inv_root[:, :], hist["dst"][:, 0:NT], 1.0, None, ALU.add))
                dve.sem_inc(sm["pe_ready"], 1)
                c.link(v.tensor_tensor_scan(scan[:, :], one_row[:, :], hist["src"][:, 0:NT], 0.0, ALU.mult, ALU.add))
                c.link(v.tensor_tensor(run[:, :], scan[:, :], hist["src"][:, 0:NT], ALU.subtract))
                dve.sem_inc(sm["pe_ready"], 1)
                dve.wait_ge(sm["rooted"], 1)
                c.link(v.reciprocal(k.inv_root[:, :], k.inv_root[:, :]))
                dve.wait_ge(sm["offset"], 1)
                c.link(v.tensor_copy(offset[:, :], off[:, 0:1]))
                c.link(v.tensor_scalar(run[:, :], run[:, :], offset[:, 0:1], None, ALU.add))
                dve.sem_inc(sm["pe_ready"], 1)

                dve.sem_inc(sm["ranked"], AHEAD)
                with dve.Fori(0, GROUPS // 2) as i:
                    for u in range(2):
                        g = i * 2 + u
                        dve.wait_ge(sm["used"], g + (GROUPS + 1))
                        for q in range(Q):
                            at = i * (2 * Q) + u * Q + q
                            v.tensor_scalar(lo_f[:, u, q, :], k.iota[:, 0:P], lo["src"][:, ds(at, 1)], None, ALU.is_equal)
                            v.tensor_scalar(hot_lo[:, u, 0, q, :], k.iota[:, 0:P], lo["src"][:, ds(at, 1)], None, ALU.is_equal)
                            last = v.tensor_scalar(hot_hi[:, u, 0, q, :], k.iota[:, 0:NT], hi["src"][:, ds(at, 1)], None, ALU.is_equal)
                        last.then_inc(sm["hot"], 1)
                        dve.wait_ge(sm[f"row{u}"], i * 16 + 16)
                        for q in range(Q):
                            at = i * (2 * Q) + u * Q + q
                            last = v.scalar_tensor_tensor(rank_sink[:, q, 0:P * (q + 1)], src_row[:, u, 0:P * (q + 1)], src_f[:, ds(at, 1)],
                                                          earlier[:, q, 0:P * (q + 1)], ALU.is_equal, ALU.mult,
                                                          accum_out=rank[:, u, q:q + 1])
                        last.then_inc(sm["ranked"], 1)
                        dve.wait_ge(sm["looked"], g + 1)
                        for q in range(Q):
                            last = v.tensor_tensor_reduce(out=look_sink[:, q, :], in0=look[q][:, 0:NT], in1=hot_hi[:, u, 0, q, :],
                                                          scale=1.0, scalar=0.0, op0=ALU.mult, op1=ALU.add,
                                                          accum_out=base[:, u, q:q + 1])
                        last.then_inc(sm["looks_free"], 1)
                        dve.wait_ge(sm["looks_free"], g + 1)
                        dve.wait_ge(sm["ranked"], g + 3)
                        v.tensor_tensor(pos_f[:, ds(i * (2 * Q) + u * Q, Q)], base[:, u, :], rank[:, u, :], ALU.add).then_inc(sm["moved"], 1)
                        dve.wait_ge(sm["table"], g + 1)
                        v.tensor_tensor(run[:, :], run[:, :], hist["dst"][:, 0:NT], ALU.add).then_inc(sm["pe_ready"], 1)
                dve.wait_ge(sm["moved"], GROUPS)
                v.tensor_copy(k.pos_i[:, :], pos_f[:, :]).then_inc(sm["c"], 1)

            @block.scalar
            def _(act):
                act.wait_ge(sm["pe_ready"], 1)
                nc.scalar.activation(k.inv_root[:, :], k.inv_root[:, :], ACT.Sqrt).then_inc(sm["rooted"], 1)
                act.sem_inc(sm["copied"], AHEAD)
                with act.Fori(0, GROUPS) as g:
                    act.wait_ge(sm["turned"], g + 1)
                    for u in range(1):
                        act.wait_ge(sm["used"], g + (GROUPS + 2))
                        nc.scalar.activation(loT[:, 0, :, :], turn[:, :, :], ACT.Copy).then_inc(sm["copied"], 1)

            @block.sync
            def _(sp):
                with sp.Fori(0, GROUPS // 2) as i:
                    for u in range(2):
                        sp.wait_ge(sm["ranked"], i * 2 + u + 1)
                        sp.dma_start(src_row[:, u, :], ins["src_rows"][:, ds((i * 2 + u) * (Q * P), Q * P)].to_broadcast([P, Q * P]))\
                          .then_inc(sm[f"row{u}"], 16)

            @block.tensor
            def _(pe):
                t = nc.tensor
                pe.wait_ge(sm["split"], 1)
                for name in ("dst", "src"):
                    t.matmul(hist[name][:, 0:NT], zeros[:, 0:P], zeros[:, :], start=True, stop=False)
                with pe.Fori(0, GROUPS // 2) as i:
                    for u in range(2):
                        pe.wait_ge(sm["hot"], i * 2 + u + 1)
                        for w, name in enumerate(("dst", "src")):
                            for q in range(Q):
                                last = t.matmul(hist[name][:, 0:NT], hot_lo[:, u, w, q, :], hot_hi[:, u, w, q, :], start=False, stop=False)
                        last.then_inc(sm["used"], 1)
                for name in ("dst", "src"):
                    last = t.matmul(hist[name][:, 0:NT], zeros[:, 0:P], zeros[:, :], start=False, stop=True)
                last.then_inc(sm["hist"], 1)
                pe.wait_ge(sm["pe_ready"], 2)
                t.matmul(off[:, 0:1], below[:, :], scan[:, NT - 1:NT], start=True, stop=True).then_inc(sm["offset"], 1)

                with pe.Fori(0, GROUPS // 2) as i:
                    for u in range(2):
                        g = i * 2 + u
                        pe.wait_ge(sm["hot"], g + (GROUPS + 1))
                        for q in range(Q):
                            last = t.transpose(turn[:, q, :], lo_f[:, u, q, :], k.ident[:, :])
                        last.then_inc(sm["turned"], 1)
                        pe.wait_ge(sm["copied"], g + 3)
                        pe.wait_ge(sm["pe_ready"], g + 3)
                        for q in range(Q):
                            last = t.matmul(look[q][:, 0:NT], loT[:, 0, q, :], run[:, :], start=True, stop=True)
                        last.then_inc(sm["looked"], 1)
                        for q in range(Q):
                            last = t.matmul(hist["dst"][:, 0:NT], hot_lo[:, u, 0, q, :], hot_hi[:, u, 0, q, :], start=q == 0, stop=q == Q - 1)
                        last.then_inc(sm["table"], 1)
                        pe.wait_ge(sm["looks_free"], g + 1)
                        pe.sem_inc(sm["used"], 1)
        end_phase(nc, sm)


def normalise_steps(nc, sm, dve, z, stats, mv, std, u, g, chain_wait):
    v = nc.vector
    for q in range(Q):
        last = v.bn_stats(stats[:, u, q, :], z(q))
    last.then_inc(sm["stats"], 1)
    dve.wait_ge(sm["stats"], chain_wait)
    dve.sem_inc(sm["passed"], 1)
    for q in range(Q):
        last = v.bn_aggr(mv[:, u, q, :], stats[:, u, q, :])
    last.then_inc(sm["moments"], 1)


def node_phase(nc, k, name, out, mix, self_rows=None, residual=None, weights=(), bias=None, finish="norm",
               scaled_out=None, ins=None):
    PAIRS = GROUPS // 2
    products = mix != "sum"
    norm = finish == "norm"
    two = mix == "mean"
    sm = phase(nc, name, ["w", "sums0", "sums1", "self0", "self1", "res0", "res1", "diag", "turned", "copied", "product",
                          "added", "stats", "moments", "rooted", "recip", "normed", "written0", "written1", "scaled", "done", "passed"])
    scale = {"mean": k.inv_deg, "gcn": k.inv_root}.get(mix)
    with ExitStack() as ctx:
        def sb(nm, shape, dt=F32):
            return ctx.enter_context(nc.sbuf_tensor(f"{name}_{nm}", shape, dt))

        def pb(nm, shape):
            return ctx.enter_context(nc.psum_tensor(f"{name}_{nm}", shape, F32))

        sums = sb("sums", [P, 2, Q, C])
        own = sb("own", [P, 2, Q, C])
        res = sb("res", [P, 2, Q, C])
        z = sb("z", [P, 2, Q, C])
        stats = sb("stats", [P, 2, Q, 6])
        mv = sb("mv", [P, 2, Q, 2])
        std = sb("std", [P, 2, Q])
        rstd = sb("rstd", [P, 2, Q])
        o = sb("o", [P, 2, Q, C])
        o2 = sb("o2", [P, 2, Q, C])
        eps = sb("eps", [P, 1])
        if products:
            diag = sb("diag", [P, 2, Q, P])
            sumsT = sb("sumsT", [P, 2, Q, P])
            ownT = sb("ownT", [P, 2, Q, P])
            w = [sb(f"w{i}", [C, C]) for i in range(len(weights))]
            b_row = sb("b_row", [1, C])
            pSums = [pb(f"pSums{u}", [P, Q, P]) for u in range(2)]
            pOwn = [pb(f"pOwn{u}", [P, Q, P]) for u in range(2)]
            pOut = [pb(f"pOut{u}", [P, Q, C]) for u in range(2)]
        loads_w = 16 * (len(weights) + 1) if products else 0

        with nc.Block() as block:
            @block.sync
            def _(sp):
                if products:
                    for wt, src in zip(w, weights):
                        sp.dma_start(wt[:, :], src).then_inc(sm["w"], 16)
                    sp.dma_start(b_row[:, :], bias).then_inc(sm["w"], 16)
                regs = [sp.alloc_register(f"{name}_last{q}") for q in range(Q)]
                with sp.Fori(0, PAIRS) as i:
                    for u in range(2):
                        g = i * 2 + u
                        sp.wait_ge(sm["turned"] if products else sm["added"], g + 1)
                        sp.reg_load(regs, k.last_step_i[0:1, ds(g * Q, Q)])
                        for q in range(Q):
                            step = sp.snap(regs[q], min_val=0, max_val=STEPS - 1)
                            sp.dma_start(sums[:, u, q, :], k.partial[ds(step * P, P), :]).then_inc(sm[f"sums{u}"], 16)
                        if self_rows is not None:
                            sp.dma_start(own[:, u, :, :], rows_of(self_rows, g)).then_inc(sm[f"self{u}"], 16)

            @block.gpsimd
            def _(pool):
                pool.sem_inc(sm["done"], AHEAD)
                with pool.Fori(0, PAIRS) as i:
                    for u in range(2):
                        g = i * 2 + u
                        if products and scale is not None:
                            pool.wait_ge(sm["turned"], g + 1)
                            pool.sem_inc(sm["done"], 1)
                            for q in range(Q):
                                last = nc.gpsimd.tensor_tensor(diag[:, u, q, :], k.ident[:, :],
                                                               scale[:, ds(g * Q + q, 1)].to_broadcast([P, P]), ALU.mult)
                            last.then_inc(sm["diag"], 1)
                        if residual is not None:
                            pool.wait_ge(sm["added"], g + 1)
                            pool.sem_inc(sm["done"], 1)
                            pool.dma_start(res[:, u, :, :], rows_of(residual, g)).then_inc(sm[f"res{u}"], 16)

            @block.tensor
            def _(pe):
                if not products:
                    return
                t = nc.tensor
                pe.sem_inc(sm["turned"], AHEAD)
                pe.sem_inc(sm["product"], AHEAD)
                pe.wait_ge(sm["w"], loads_w)
                with pe.Fori(0, PAIRS) as i:
                    for u in range(2):
                        g = i * 2 + u
                        pe.wait_ge(sm[f"sums{u}"], i * (16 * Q) + 16 * Q)
                        if self_rows is not None:
                            pe.wait_ge(sm[f"self{u}"], i * 16 + 16)
                        if scale is not None:
                            pe.wait_ge(sm["diag"], g + 1)
                        pe.wait_ge(sm["copied"], g + 1)
                        for q in range(Q):
                            if mix == "plain":
                                last = t.transpose(pSums[u][:, q, :], sums[:, u, q, :], k.ident[:, :])
                            else:
                                last = t.matmul(pSums[u][:, q, :], sums[:, u, q, :], diag[:, u, q, :], start=True, stop=mix == "mean")
                            if mix == "gcn":
                                last = t.matmul(pSums[u][:, q, :], own[:, u, q, :], diag[:, u, q, :], start=False, stop=True)
                            if two:
                                last = t.transpose(pOwn[u][:, q, :], own[:, u, q, :], k.ident[:, :])
                        last.then_inc(sm["turned"], 1)
                    for u in range(2):
                        g = i * 2 + u
                        pe.wait_ge(sm["copied"], g + 3)
                        pe.wait_ge(sm["added"], g + 1)
                        for q in range(Q):
                            t.matmul(pOut[u][:, q, :], k.ones[0:1, :], b_row[0:1, :], start=True, stop=False)
                            if two:
                                t.matmul(pOut[u][:, q, :], ownT[:, u, q, :], w[1][:, :], start=False, stop=False)
                            last = t.matmul(pOut[u][:, q, :], sumsT[:, u, q, :], w[0][:, :], start=False, stop=True)
                        last.then_inc(sm["product"], 1)

            @block.scalar
            def _(act):
                a = nc.scalar
                act.sem_inc(sm["copied"], AHEAD)
                act.sem_inc(sm["rooted"], AHEAD)
                act.sem_inc(sm["written0"], 16)
                act.sem_inc(sm["written1"], 16)
                if not norm:
                    act.sem_inc(sm["added"], AHEAD)

                def write(i, u):
                    act.dma_start(rows_of(out, i * 2 + u), o[:, u, :, :]).then_inc(sm[f"written{u}"], 16)
                    if norm and scaled_out is not None:
                        act.dma_start(rows_of(scaled_out, i * 2 + u), o2[:, u, :, :]).then_inc(sm[f"written{u}"], 16)

                with act.Fori(0, PAIRS) as i:
                    for u in range(2):
                        g = i * 2 + u
                        if products:
                            act.wait_ge(sm["turned"], g + 3)
                            act.wait_ge(sm["product"], g + 1)
                            if two:
                                a.activation(ownT[:, u, :, :], pOwn[u][:, :, :], ACT.Copy)
                            a.activation(sumsT[:, u, :, :], pSums[u][:, :, :], ACT.Copy).then_inc(sm["copied"], 1)
                    for u in range(2):
                        g = i * 2 + u
                        if norm:
                            act.wait_ge(sm["moments"], g + 1)
                            act.wait_ge(sm["recip"], g + 1)
                            a.activation(std[:, u, :], mv[:, u, :, 1], ACT.Sqrt, bias=eps[:, 0:1]).then_inc(sm["rooted"], 1)
                        else:
                            act.wait_ge(sm["product"], g + 3)
                            act.wait_ge(sm[f"written{u}"], i * 16 + 16)
                            if scaled_out:
                                for q in range(Q):
                                    last = a.activation(o[:, u, q, :], pOut[u][:, q, :], ACT.Relu, scale=scale[:, ds(g * Q + q, 1)])
                            else:
                                last = a.activation(o[:, u, :, :], pOut[u][:, :, :], ACT.Relu)
                            last.then_inc(sm["added"], 1)
                    for u in range(2):
                        g = i * 2 + u
                        act.wait_ge(sm["normed"] if norm else sm["added"], (g + 1) if norm else (g + 3))
                        write(i, u)
                per = 32 if norm and scaled_out is not None else 16
                for u in range(2):
                    act.wait_ge(sm[f"written{u}"], 16 + per * PAIRS)

            @block.vector
            def _(dve):
                if not norm:
                    return
                v = nc.vector
                v.memset(eps[:, :], EPS).then_inc(sm["scaled"], 1)
                dve.wait_ge(sm["scaled"], 1)
                dve.sem_inc(sm["added"], AHEAD)
                dve.sem_inc(sm["recip"], AHEAD)
                per = 32 if scaled_out is not None else 16
                with dve.Fori(0, PAIRS) as i:
                    for u in range(2):
                        g = i * 2 + u
                        if residual is not None:
                            dve.wait_ge(sm[f"res{u}"], i * 16 + 16)
                        if products:
                            dve.wait_ge(sm["product"], g + 3)
                            first = pOut[u][:, :, :]
                        else:
                            dve.wait_ge(sm[f"sums{u}"], i * (16 * Q) + 16 * Q)
                            first = sums[:, u, :, :]
                        v.tensor_tensor(z[:, u, :, :], first, res[:, u, :, :], ALU.add).then_inc(sm["added"], 1)
                        dve.wait_ge(sm["added"], g + 3)
                        normalise_steps(nc, sm, dve, lambda q: z[:, u, q, :], stats, mv, std, u, g, g + 1)
                    for u in range(2):
                        g = i * 2 + u
                        dve.wait_ge(sm["rooted"], g + 3)
                        v.reciprocal(rstd[:, u, :], std[:, u, :]).then_inc(sm["recip"], 1)
                        dve.wait_ge(sm["recip"], g + 3)
                        dve.wait_ge(sm[f"written{u}"], i * per + 16)
                        for q in range(Q):
                            last = v.tensor_scalar(o[:, u, q, :], z[:, u, q, :], mv[:, u, q, 0:1], rstd[:, u, q:q + 1],
                                                   ALU.subtract, ALU.mult)
                        if scaled_out is not None:
                            last.then_inc(sm["scaled"], 1)
                            dve.wait_ge(sm["scaled"], g + 2)
                            for q in range(Q):
                                last = v.tensor_scalar(o2[:, u, q, :], o[:, u, q, :], k.inv_root[:, ds(g * Q + q, 1)], None, ALU.mult)
                        last.then_inc(sm["normed"], 1)
        end_phase(nc, sm)


def edge_mlp(nc, k, ins, messages):
    PAIRS = GROUPS // 2
    sm = phase(nc, "mlp", ["w", "rows", "pass_pool", "src0", "src1", "dst0", "dst1", "turned", "copied_src", "copied_dst",
                           "prod1", "stats1", "moments1", "rooted1", "recip1", "normed1", "turned2", "affine1", "slanted1",
                           "prod2", "stats2", "moments2", "rooted2", "recip2", "normed2", "gained", "affine2", "slanted2",
                           "weighted", "written0", "written1", "eps", "passed"])
    x = ins["x"]
    with ExitStack() as ctx:
        def sb(nm, shape, dt=F32):
            return ctx.enter_context(nc.sbuf_tensor(f"mlp_{nm}", shape, dt))

        def pb(nm):
            return [ctx.enter_context(nc.psum_tensor(f"mlp_{nm}{u}", [P, Q, P], F32)) for u in range(2)]

        w1a, w1b, w2 = sb("w1a", [C, C]), sb("w1b", [C, C]), sb("w2", [C, C])
        b1, b2 = sb("b1", [1, C]), sb("b2", [1, C])
        g1, be1 = sb("g1", [C, 1]), sb("be1", [C, 1])
        g2, be2 = sb("g2", [P, C]), sb("be2", [P, C])
        rows = sb("rows", [P, 2, 2, Q], I32)
        xs, xd = sb("xs", [P, 2, Q, C]), sb("xd", [P, 2, Q, C])
        xsT, xdT = sb("xsT", [P, 2, Q, P]), sb("xdT", [P, 2, Q, P])
        t1 = sb("t1", [P, 2, Q, P])
        h, h1T = sb("h", [P, 2, Q, C]), sb("h1T", [P, 2, Q, P])
        h2, h3, m = sb("h2", [P, 2, Q, C]), sb("h3", [P, 2, Q, C]), sb("m", [P, 2, Q, C])
        stats, mv = sb("stats", [P, 2, Q, 6]), sb("mv", [P, 2, Q, 2])
        stats_b, mv_b = sb("stats_b", [P, 2, Q, 6]), sb("mv_b", [P, 2, Q, 2])
        std, rstd = sb("std", [P, 2, 2, Q]), sb("rstd", [P, 2, 2, Q])
        eps = sb("eps", [P, 1])
        pSrc, pDst, pH, pT = pb("pSrc"), pb("pDst"), pb("pH"), pb("pT")

        with nc.Block() as block:
            @block.sync
            def _(sp):
                sp.dma_start(w1a[:, :], ins["L0_gnn_w1"][0:C, :]).then_inc(sm["w"], 16)
                sp.dma_start(w1b[:, :], ins["L0_gnn_w1"][C:2 * C, :]).then_inc(sm["w"], 16)
                sp.dma_start(w2[:, :], ins["L0_gnn_w2"]).then_inc(sm["w"], 16)
                sp.dma_start(b1[:, :], ins["L0_gnn_b1"]).then_inc(sm["w"], 16)
                sp.dma_start(b2[:, :], ins["L0_gnn_b2"]).then_inc(sm["w"], 16)
                sp.dma_start(g1[:, :], ins["L0_gnn_g1"].rearrange("a c -> c a")).then_inc(sm["w"], 16)
                sp.dma_start(be1[:, :], ins["L0_gnn_be1"].rearrange("a c -> c a")).then_inc(sm["w"], 16)
                sp.dma_start(g2[:, :], ins["L0_gnn_g2"].to_broadcast([P, C])).then_inc(sm["w"], 16)
                sp.dma_start(be2[:, :], ins["L0_gnn_be2"].to_broadcast([P, C])).then_inc(sm["w"], 16)
                sp.sem_inc(sm["written0"], 16)
                sp.sem_inc(sm["written1"], 16)
                with sp.Fori(0, PAIRS) as i:
                    for u in range(2):
                        sp.wait_ge(sm["weighted"], i * 2 + u + 3)
                        sp.dma_start(rows_of(messages, i * 2 + u), m[:, u, :, :]).then_inc(sm[f"written{u}"], 16)
                for u in range(2):
                    sp.wait_ge(sm[f"written{u}"], 16 + 16 * PAIRS)

            @block.gpsimd
            def _(pool):
                with pool.Fori(0, PAIRS) as i:
                    for u in range(2):
                        g = i * 2 + u
                        pool.wait_ge(sm["turned"], g + 1)
                        pool.sem_inc(sm["pass_pool"], 1)
                        nc.gpsimd.tensor_copy(rows[:, u, 0, :], k.src_i[:, ds(g * Q, Q)])
                        nc.gpsimd.tensor_copy(rows[:, u, 1, :], k.dst_row[:, ds(g * Q, Q)]).then_inc(sm["rows"], 1)
                        pool.wait_ge(sm["rows"], g + 1)
                        pool.sem_inc(sm["pass_pool"], 1)
                        for w, (to, sem) in enumerate(((xs, "src"), (xd, "dst"))):
                            for q in range(Q):
                                pool.indirect_dma_start(to[:, u, q, :], None, x[:, :], bass.IndirectOffsetOnAxis(
                                    ap=rows[:, u, w, q:q + 1], axis=0)).then_inc(sm[f"{sem}{u}"], 16)

            @block.tensor
            def _(pe):
                t = nc.tensor
                pe.sem_inc(sm["turned"], AHEAD)
                pe.sem_inc(sm["prod1"], AHEAD)
                pe.sem_inc(sm["turned2"], AHEAD)
                pe.sem_inc(sm["prod2"], AHEAD)
                pe.wait_ge(sm["w"], 16 * 9)
                with pe.Fori(0, PAIRS) as i:
                    for u in range(2):
                        g = i * 2 + u
                        pe.wait_ge(sm[f"src{u}"], i * (16 * Q) + 16 * Q)
                        pe.wait_ge(sm[f"dst{u}"], i * (16 * Q) + 16 * Q)
                        pe.wait_ge(sm["copied_src"], g + 1)
                        pe.wait_ge(sm["copied_dst"], g + 1)
                        for q in range(Q):
                            t.transpose(pSrc[u][:, q, :], xs[:, u, q, :], k.ident[:, :])
                            last = t.transpose(pDst[u][:, q, :], xd[:, u, q, :], k.ident[:, :])
                        last.then_inc(sm["turned"], 1)
                    for u in range(2):
                        g = i * 2 + u
                        pe.wait_ge(sm["copied_src"], g + 3)
                        pe.wait_ge(sm["copied_dst"], g + 3)
                        pe.wait_ge(sm["normed2"], g + 1)
                        for q in range(Q):
                            t.matmul(pH[u][:, q, :], k.ones[0:1, :], b1[0:1, :], start=True, stop=False)
                            t.matmul(pH[u][:, q, :], xsT[:, u, q, :], w1a[:, :], start=False, stop=False)
                            last = t.matmul(pH[u][:, q, :], xdT[:, u, q, :], w1b[:, :], start=False, stop=True)
                        last.then_inc(sm["prod1"], 1)
                    for u in range(2):
                        g = i * 2 + u
                        pe.wait_ge(sm["normed1"], g + 3)
                        pe.wait_ge(sm["affine1"], g + 1)
                        for q in range(Q):
                            last = t.transpose(pT[u][:, q, :], h[:, u, q, :], k.ident[:, :])
                        last.then_inc(sm["turned2"], 1)
                    for u in range(2):
                        g = i * 2 + u
                        pe.wait_ge(sm["slanted1"], g + 3)
                        for q in range(Q):
                            t.matmul(pH[u][:, q, :], k.ones[0:1, :], b2[0:1, :], start=True, stop=False)
                            last = t.matmul(pH[u][:, q, :], h1T[:, u, q, :], w2[:, :], start=False, stop=True)
                        last.then_inc(sm["prod2"], 1)

            @block.scalar
            def _(act):
                a = nc.scalar
                for s in ("copied_src", "affine1", "rooted1", "rooted2", "weighted"):
                    act.sem_inc(sm[s], AHEAD)
                act.wait_ge(sm["w"], 16 * 9)
                act.wait_ge(sm["eps"], 1)
                with act.Fori(0, PAIRS) as i:
                    for u in range(2):
                        g = i * 2 + u
                        act.wait_ge(sm["turned"], g + 3)
                        act.wait_ge(sm["prod1"], g + 1)
                        a.activation(xsT[:, u, :, :], pSrc[u][:, :, :], ACT.Copy).then_inc(sm["copied_src"], 1)
                    for u in range(2):
                        g = i * 2 + u
                        act.wait_ge(sm["moments1"], g + 1)
                        a.activation(std[:, u, 0, :], mv[:, u, :, 1], ACT.Sqrt, bias=eps[:, 0:1]).then_inc(sm["rooted1"], 1)
                    for u in range(2):
                        g = i * 2 + u
                        act.wait_ge(sm["turned2"], g + 3)
                        act.wait_ge(sm["slanted1"], g + 1)
                        a.activation(t1[:, u, :, :], pT[u][:, :, :], ACT.Identity, scale=g1[:, 0:1], bias=be1[:, 0:1])\
                         .then_inc(sm["affine1"], 1)
                    for u in range(2):
                        g = i * 2 + u
                        act.wait_ge(sm["moments2"], g + 1)
                        a.activation(std[:, u, 1, :], mv_b[:, u, :, 1], ACT.Sqrt, bias=eps[:, 0:1]).then_inc(sm["rooted2"], 1)
                    for u in range(2):
                        g = i * 2 + u
                        act.wait_ge(sm["slanted2"], g + 1)
                        act.wait_ge(sm[f"written{u}"], i * 16 + 16)
                        for q in range(Q):
                            last = a.activation(m[:, u, q, :], h3[:, u, q, :], ACT.Copy, scale=k.ew[:, ds(g * Q + q, 1)])
                        last.then_inc(sm["weighted"], 1)

            @block.vector
            def _(dve):
                v = nc.vector
                v.memset(eps[:, :], EPS).then_inc(sm["eps"], 1)
                for s in ("copied_dst", "normed1", "normed2", "slanted1"):
                    dve.sem_inc(sm[s], AHEAD)
                dve.wait_ge(sm["w"], 16 * 9)

                def moments(g, u, bank, st, mo, which):
                    dve.wait_ge(sm[f"prod{which}"], g + 3)
                    for q in range(Q):
                        last = v.bn_stats(st[:, u, q, :], bank[:, q, :])
                    last.then_inc(sm[f"stats{which}"], 1)
                    dve.wait_ge(sm[f"stats{which}"], g + 1)
                    dve.sem_inc(sm["passed"], 1)
                    for q in range(Q):
                        last = v.bn_aggr(mo[:, u, q, :], st[:, u, q, :])
                    last.then_inc(sm[f"moments{which}"], 1)

                def normalise(g, u, bank, mo, to, which):
                    dve.wait_ge(sm[f"rooted{which}"], g + 3)
                    v.reciprocal(rstd[:, u, which - 1, :], std[:, u, which - 1, :]).then_inc(sm[f"recip{which}"], 1)
                    dve.wait_ge(sm[f"recip{which}"], g + 1)
                    for q in range(Q):
                        last = v.tensor_scalar(to[:, u, q, :], bank[:, q, :], mo[:, u, q, 0:1], rstd[:, u, which - 1, q:q + 1],
                                               ALU.subtract, ALU.mult)
                    last.then_inc(sm[f"normed{which}"], 1)

                with dve.Fori(0, PAIRS) as i:
                    for u in range(2):
                        g = i * 2 + u
                        dve.wait_ge(sm["turned"], g + 3)
                        dve.wait_ge(sm["prod1"], g + 1)
                        v.tensor_copy(xdT[:, u, :, :], pDst[u][:, :, :]).then_inc(sm["copied_dst"], 1)
                    for u in range(2):
                        moments(i * 2 + u, u, pH[u], stats, mv, 1)
                    for u in range(2):
                        dve.wait_ge(sm["turned2"], i * 2 + u + 1)
                        normalise(i * 2 + u, u, pH[u], mv, h, 1)
                    for u in range(2):
                        g = i * 2 + u
                        dve.wait_ge(sm["affine1"], g + 3)
                        dve.wait_ge(sm["prod2"], g + 1)
                        v.scalar_tensor_tensor(h1T[:, u, :, :], t1[:, u, :, :], SLOPE, t1[:, u, :, :], ALU.mult, ALU.max)\
                         .then_inc(sm["slanted1"], 1)
                    for u in range(2):
                        moments(i * 2 + u, u, pH[u], stats_b, mv_b, 2)
                    for u in range(2):
                        g = i * 2 + u
                        normalise(g, u, pH[u], mv_b, h2, 2)
                        dve.wait_ge(sm["normed2"], g + 3)
                        v.tensor_tensor(h2[:, u, :, :], h2[:, u, :, :], g2[:, :].unsqueeze(1).to_broadcast([P, Q, C]), ALU.mult)\
                         .then_inc(sm["gained"], 1)
                        dve.wait_ge(sm["gained"], g + 1)
                        v.tensor_tensor(h2[:, u, :, :], h2[:, u, :, :], be2[:, :].unsqueeze(1).to_broadcast([P, Q, C]), ALU.add)\
                         .then_inc(sm["affine2"], 1)
                        dve.wait_ge(sm["affine2"], g + 1)
                        dve.wait_ge(sm["weighted"], g + 1)
                        v.scalar_tensor_tensor(h3[:, u, :, :], h2[:, u, :, :], SLOPE, h2[:, u, :, :], ALU.mult, ALU.max)\
                         .then_inc(sm["slanted2"], 1)
        end_phase(nc, sm)


def project(nc, k, ins, x3, qv, keys):
    PAIRS = GROUPS // 2
    sm = phase(nc, "proj", ["w", "in0", "in1", "turned", "copied", "product", "taken_act", "taken_dve", "pass_pool", "written0", "written1"])
    W = 3 * C
    with ExitStack() as ctx:
        def sb(nm, shape, dt=F32):
            return ctx.enter_context(nc.sbuf_tensor(f"proj_{nm}", shape, dt))

        w, b = sb("w", [C, W]), sb("b", [1, W])
        x, xT, o = sb("x", [P, 2, Q, C]), sb("xT", [P, 2, Q, P]), sb("o", [P, 2, Q, W])
        pT = [ctx.enter_context(nc.psum_tensor(f"proj_pT{u}", [P, Q, P], F32)) for u in range(2)]
        pO = [ctx.enter_context(nc.psum_tensor(f"proj_pO{q}", [P, 512], F32)) for q in range(Q)]

        with nc.Block() as block:
            @block.sync
            def _(sp):
                for j, n in enumerate("qvk"):
                    sp.dma_start(w[:, j * C:(j + 1) * C], ins[f"L3_gnn_W{n}"]).then_inc(sm["w"], 16)
                    sp.dma_start(b[:, j * C:(j + 1) * C], ins[f"L3_gnn_b{n}"]).then_inc(sm["w"], 16)
                sp.sem_inc(sm["written0"], 32)
                sp.sem_inc(sm["written1"], 32)
                with sp.Fori(0, PAIRS) as i:
                    for u in range(2):
                        g = i * 2 + u
                        sp.wait_ge(sm["taken_act"], g + 2)
                        sp.wait_ge(sm["taken_dve"], g + 2)
                        sp.dma_start(rows_of(qv, g), o[:, u, :, 0:2 * C]).then_inc(sm[f"written{u}"], 16)
                        sp.dma_start(rows_of(keys, g), o[:, u, :, 2 * C:W]).then_inc(sm[f"written{u}"], 16)
                for u in range(2):
                    sp.wait_ge(sm[f"written{u}"], 32 + 32 * PAIRS)

            @block.gpsimd
            def _(pool):
                with pool.Fori(0, PAIRS) as i:
                    for u in range(2):
                        pool.wait_ge(sm["turned"], i * 2 + u + 1)
                        pool.sem_inc(sm["pass_pool"], 1)
                        pool.dma_start(x[:, u, :, :], rows_of(x3, i * 2 + u)).then_inc(sm[f"in{u}"], 16)

            @block.tensor
            def _(pe):
                t = nc.tensor
                pe.sem_inc(sm["turned"], AHEAD)
                pe.sem_inc(sm["product"], AHEAD)
                pe.wait_ge(sm["w"], 96)

                with pe.Fori(0, PAIRS) as i:
                    for u in range(2):
                        pe.wait_ge(sm[f"in{u}"], i * 16 + 16)
                        pe.wait_ge(sm["copied"], i * 2 + u + 1)
                        for q in range(Q):
                            last = t.transpose(pT[u][:, q, :], x[:, u, q, :], k.ident[:, :])
                        last.then_inc(sm["turned"], 1)
                    for u in range(2):
                        g = i * 2 + u
                        pe.wait_ge(sm["copied"], g + 3)
                        pe.wait_ge(sm["taken_dve"], g + 1)
                        pe.wait_ge(sm["taken_act"], g + 1)
                        for q in range(Q):
                            t.matmul(pO[q][:, 0:W], k.ones[0:1, :], b[0:1, :], start=True, stop=False)
                            last = t.matmul(pO[q][:, 0:W], xT[:, u, q, :], w[:, :], start=False, stop=True)
                        last.then_inc(sm["product"], 1)

            @block.scalar
            def _(act):
                act.sem_inc(sm["copied"], AHEAD)
                act.sem_inc(sm["taken_act"], 1)
                with act.Fori(0, PAIRS) as i:
                    for u in range(2):
                        g = i * 2 + u
                        act.wait_ge(sm["turned"], g + 3)
                        act.wait_ge(sm["product"], g + 1)
                        nc.scalar.activation(xT[:, u, :, :], pT[u][:, :, :], ACT.Copy).then_inc(sm["copied"], 1)
                    for u in range(2):
                        g = i * 2 + u
                        act.wait_ge(sm["product"], g + 3)
                        act.wait_ge(sm[f"written{u}"], i * 32 + 32)
                        nc.scalar.activation(o[:, u, 2, :], pO[2][:, 0:W], ACT.Copy)
                        nc.scalar.activation(o[:, u, 3, :], pO[3][:, 0:W], ACT.Copy).then_inc(sm["taken_act"], 1)

            @block.vector
            def _(dve):
                dve.sem_inc(sm["taken_dve"], 1)
                with dve.Fori(0, PAIRS) as i:
                    for u in range(2):
                        g = i * 2 + u
                        dve.wait_ge(sm["product"], g + 3)
                        dve.wait_ge(sm[f"written{u}"], i * 32 + 32)
                        nc.vector.tensor_copy(o[:, u, 0, :], pO[0][:, 0:W])
                        nc.vector.tensor_copy(o[:, u, 1, :], pO[1][:, 0:W]).then_inc(sm["taken_dve"], 1)
        end_phase(nc, sm)


ROW = HEADS + 1


def edge_scores(nc, k, ins, qv, keys, values, by_source):
    PAIRS = GROUPS // 2
    sm = phase(nc, "score", ["mask", "rows", "pass_pool", "qv0", "qv1", "k0", "k1", "multiplied", "reduced", "scored",
                             "kept0", "kept1", "scattered0", "scattered1"])
    with ExitStack() as ctx:
        def sb(nm, shape, dt=F32):
            return ctx.enter_context(nc.sbuf_tensor(f"score_{nm}", shape, dt))

        mask = sb("mask", [P, ET, HEADS])
        src_f = sb("src_f", [P, ET])
        rows = sb("rows", [P, 2, 3, Q], I32)
        q_and_v = sb("q_and_v", [P, 2, Q, 2 * C])
        key = sb("key", [P, 2, Q, C])
        prod = sb("prod", [P, 2, Q, C])
        dots = sb("dots", [P, 2, Q, HEADS])
        line = sb("line", [P, 2, Q, ROW])

        with nc.Block() as block:
            @block.sync
            def _(sp):
                sp.dma_start(mask[:, :, :], ins["mask"].rearrange("p (t h) -> p t h", h=HEADS)).then_inc(sm["mask"], 16)
                sp.sem_inc(sm["kept0"], 16)
                sp.sem_inc(sm["kept1"], 16)
                with sp.Fori(0, PAIRS) as i:
                    for u in range(2):
                        sp.wait_ge(sm[f"qv{u}"], i * (16 * Q) + 16 * Q)
                        sp.dma_start(rows_of(values, i * 2 + u), q_and_v[:, u, :, C:2 * C]).then_inc(sm[f"kept{u}"], 16)
                for u in range(2):
                    sp.wait_ge(sm[f"kept{u}"], 16 + 16 * PAIRS)

            @block.gpsimd
            def _(pool):
                def pair(i, first=False):
                    for u in range(2):
                        g = i * 2 + u
                        pool.wait_ge(sm["scored"], g + 1)
                        pool.wait_ge(sm[f"kept{u}"], i * 16 + 16)
                        if not first:
                            pool.wait_ge(sm[f"scattered{u}"], i * (16 * Q))
                        pool.sem_inc(sm["pass_pool"], 1)
                        for w, idx in enumerate((k.src_i, k.dst_row, k.pos_i)):
                            last = nc.gpsimd.tensor_copy(rows[:, u, w, :], idx[:, ds(g * Q, Q)])
                        last.then_inc(sm["rows"], 1)
                        pool.wait_ge(sm["rows"], g + 1)
                        pool.sem_inc(sm["pass_pool"], 1)
                        for q in range(Q):
                            pool.indirect_dma_start(q_and_v[:, u, q, :], None, qv[:, :], bass.IndirectOffsetOnAxis(
                                ap=rows[:, u, 0, q:q + 1], axis=0)).then_inc(sm[f"qv{u}"], 16)
                            pool.indirect_dma_start(key[:, u, q, :], None, keys[:, :], bass.IndirectOffsetOnAxis(
                                ap=rows[:, u, 1, q:q + 1], axis=0)).then_inc(sm[f"k{u}"], 16)
                    for u in range(2):
                        g = i * 2 + u
                        pool.wait_ge(sm["scored"], g + 3)
                        pool.sem_inc(sm["pass_pool"], 1)
                        for q in range(Q):
                            pool.indirect_dma_start(by_source[:, :], bass.IndirectOffsetOnAxis(ap=rows[:, u, 2, q:q + 1], axis=0),
                                                    line[:, u, q, :], None).then_inc(sm[f"scattered{u}"], 16)

                pair(0, first=True)
                with pool.Fori(1, PAIRS) as i:
                    pair(i)
                for u in range(2):
                    pool.wait_ge(sm[f"scattered{u}"], 16 * Q * PAIRS)

            @block.vector
            def _(dve):
                v = nc.vector
                v.tensor_copy(src_f[:, :], k.src_i[:, :]).then_inc(sm["multiplied"], 1)
                dve.sem_inc(sm["scored"], AHEAD)
                dve.wait_ge(sm["multiplied"], 1)
                dve.wait_ge(sm["mask"], 16)
                with dve.Fori(0, PAIRS) as i:
                    for u in range(2):
                        g = i * 2 + u
                        dve.wait_ge(sm[f"qv{u}"], i * (16 * Q) + 16 * Q)
                        dve.wait_ge(sm[f"k{u}"], i * (16 * Q) + 16 * Q)
                        v.tensor_tensor(prod[:, u, :, :], q_and_v[:, u, :, 0:C], key[:, u, :, :], ALU.mult).then_inc(sm["multiplied"], 1)
                        dve.wait_ge(sm["multiplied"], g + 2)
                        v.reduce_sum(dots[:, u, :, :], prod[:, u, :, :].rearrange("p q (h d) -> p q h d", h=HEADS), AX_X)\
                         .then_inc(sm["reduced"], 1)
                        dve.wait_ge(sm["reduced"], g + 1)
                        v.tensor_copy(line[:, u, :, HEADS:ROW], src_f[:, ds(g * Q, Q)].unsqueeze(2))
                        v.scalar_tensor_tensor(line[:, u, :, 0:HEADS], dots[:, u, :, :], float(DH) ** -0.5, mask[:, ds(g * Q, Q), :],
                                               ALU.mult, ALU.add).then_inc(sm["scored"], 1)
        end_phase(nc, sm)


def softmax_by_source(nc, k, by_source, weights):
    L = NT
    BIG = 3.0e38
    sm = phase(nc, "soft", ["loaded", "dve", "pe", "to_pe", "exp", "to_act", "out"])
    with ExitStack() as ctx:
        def sb(nm, shape, dt=F32):
            return ctx.enter_context(nc.sbuf_tensor(f"soft_{nm}", shape, dt))

        line = sb("line", [P, L, ROW])
        before = sb("before", [P, ROW])
        after = sb("after", [P, ROW])
        src = sb("src", [P, L + 2])
        same = sb("same", [P, L + 1])
        pen = sb("pen", [P, L])
        whole = sb("whole", [P, 2])
        A = sb("A", [P, HEADS, L])
        B = sb("B", [P, HEADS, L])
        M = sb("M", [P, HEADS, L])
        X = sb("X", [P, HEADS, L])
        ends = sb("ends", [P, 2, HEADS])
        row = sb("row", [HEADS, 2, P])
        handed = sb("handed", [HEADS, P + 2])
        come = sb("come", [P, HEADS])
        pR = [ctx.enter_context(nc.psum_tensor(f"soft_p{j}", [P, 512], F32)) for j in range(3)]

        with nc.Block() as block:
            @block.sync
            def _(sp):
                lines = by_source.rearrange("(p j) r -> p j r", p=P)
                sp.dma_start(line[:, :, :], lines).then_inc(sm["loaded"], 16)
                sp.dma_start(before[1:P, :], lines[0:P - 1, L - 1, :]).then_inc(sm["loaded"], 16)
                sp.dma_start(after[0:P - 1, :], lines[1:P, 0, :]).then_inc(sm["loaded"], 16)
                sp.dma_start(before[0:1, :], k.no_source).then_inc(sm["loaded"], 16)
                sp.dma_start(after[P - 1:P, :], k.no_source).then_inc(sm["loaded"], 16)
                sp.wait_ge(sm["out"], 1)
                sp.dma_start(weights.rearrange("(p j) h -> p j h", p=P), line[:, :, 0:HEADS]).then_inc(sm["loaded"], 16)
                sp.wait_ge(sm["loaded"], 96)

            @block.tensor
            def _(pe):
                t = nc.tensor
                for n in range(4):
                    pe.wait_ge(sm["to_pe"], 2 * n + 1)
                    t.transpose(pR[0][0:HEADS, 0:P], ends[:, 0, :], k.ident[:, :])
                    t.transpose(pR[1][0:HEADS, 0:P], ends[:, 1, :], k.ident[:, :]).then_inc(sm["pe"], 1)
                    pe.wait_ge(sm["to_pe"], 2 * n + 2)
                    lo = 0 if n % 2 == 0 else 2
                    t.transpose(pR[2][:, 0:HEADS], handed[:, lo:lo + P], k.ident[0:HEADS, 0:HEADS]).then_inc(sm["pe"], 1)

            @block.scalar
            def _(act):
                act.wait_ge(sm["to_act"], 1)
                nc.scalar.activation(X[:, :, :], X[:, :, :], ACT.Exp).then_inc(sm["exp"], 1)

            @block.vector
            def _(dve):
                v = nc.vector
                c = Chain(dve, sm["dve"])
                dve.wait_ge(sm["loaded"], 80)
                c.link(v.tensor_copy(src[:, 1:L + 1], line[:, :, HEADS]))
                c.link(v.tensor_copy(src[:, 0:1], before[:, HEADS:ROW]))
                c.link(v.tensor_copy(src[:, L + 1:L + 2], after[:, HEADS:ROW]))
                c.link(v.tensor_tensor(same[:, :], src[:, 1:L + 2], src[:, 0:L + 1], ALU.is_equal))
                c.link(v.tensor_scalar(pen[:, :], same[:, 0:L], 1.0, BIG, ALU.subtract, ALU.mult))
                c.link(v.tensor_reduce(whole[:, 0:1], same[:, 0:L], AX_X, ALU.min))
                c.link(v.tensor_reduce(whole[:, 1:2], same[:, 1:L + 1], AX_X, ALU.min))
                turns = [0]

                def hand_over(last_column, factor, start, op0, op1, backward):
                    c.link(v.tensor_copy(ends[:, 0, :], last_column))
                    c.link(v.tensor_copy(ends[:, 1, :], factor.to_broadcast([P, HEADS])))
                    dve.sem_inc(sm["to_pe"], 1)
                    turns[0] += 1
                    dve.wait_ge(sm["pe"], turns[0])
                    c.link(v.tensor_copy(row[:, 0, :], pR[0][0:HEADS, 0:P]))
                    c.link(v.tensor_copy(row[:, 1, :], pR[1][0:HEADS, 0:P]))
                    if op1 == ALU.max:
                        c.link(v.tensor_scalar(row[:, 1, :], row[:, 1, :], 1.0, BIG, ALU.subtract, ALU.mult))
                    c.link(v.memset(handed[:, :], start))
                    if backward:
                        c.link(v.tensor_tensor_scan(handed[:, 1:P + 1][:, ::-1], row[:, 1, ::-1], row[:, 0, ::-1], start, op0, op1))
                    else:
                        c.link(v.tensor_tensor_scan(handed[:, 1:P + 1], row[:, 1, :], row[:, 0, :], start, op0, op1))
                    dve.sem_inc(sm["to_pe"], 1)
                    turns[0] += 1
                    dve.wait_ge(sm["pe"], turns[0])
                    c.link(v.tensor_copy(come[:, :], pR[2][:, 0:HEADS]))

                def forward(out, flags, values, start, op0, op1):
                    for h in range(HEADS):
                        last = v.tensor_tensor_scan(out[:, h, :], flags, values[:, h, :], start, op0, op1)
                    c.link(last)
                    hand_over(out[:, :, L - 1], whole[:, 0:1], start, op0, op1, False)
                    for h in range(HEADS):
                        last = v.tensor_tensor_scan(out[:, h, :], flags, values[:, h, :], come[:, h:h + 1], op0, op1)
                    c.link(last)

                def spread(out, values):
                    c.link(v.tensor_scalar(pen[:, :], same[:, 1:L + 1], -1.0, 1.0, ALU.mult, ALU.add))
                    c.link(v.tensor_tensor(B[:, :, :], values[:, :, :], pen[:, :].unsqueeze(1).to_broadcast([P, HEADS, L]), ALU.mult))
                    back = same[:, 1:L + 1]
                    for h in range(HEADS):
                        last = v.tensor_tensor_scan(out[:, h, ::-1], back[:, ::-1], B[:, h, ::-1], 0.0, ALU.mult, ALU.add)
                    c.link(last)
                    hand_over(out[:, :, 0], whole[:, 1:2], 0.0, ALU.mult, ALU.add, True)
                    for h in range(HEADS):
                        last = v.tensor_tensor_scan(out[:, h, ::-1], back[:, ::-1], B[:, h, ::-1], come[:, h:h + 1], ALU.mult, ALU.add)
                    c.link(last)

                c.link(v.tensor_copy(X[:, :, :], line[:, :, 0:HEADS].rearrange("p j h -> p h j")))
                forward(A, pen[:, :], X, -BIG, ALU.add, ALU.max)
                spread(M, A)
                v.tensor_tensor(X[:, :, :], X[:, :, :], M[:, :, :], ALU.subtract).then_inc(sm["to_act"], 1)
                dve.wait_ge(sm["exp"], 1)
                forward(A, same[:, 0:L], X, 0.0, ALU.mult, ALU.add)
                spread(M, A)
                c.link(v.reciprocal(M[:, :, :], M[:, :, :]))
                v.tensor_tensor(line[:, :, 0:HEADS].rearrange("p j h -> p h j"), X[:, :, :], M[:, :, :], ALU.mult).then_inc(sm["out"], 1)
        end_phase(nc, sm)


def weigh(nc, k, values, weights, messages):
    PAIRS = GROUPS // 2
    sm = phase(nc, "weigh", ["rows", "pass_pool", "w0", "w1", "v0", "v1", "weighed", "written0", "written1"])
    with ExitStack() as ctx:
        def sb(nm, shape, dt=F32):
            return ctx.enter_context(nc.sbuf_tensor(f"weigh_{nm}", shape, dt))

        rows = sb("rows", [P, 2, Q], I32)
        w, val, m = sb("w", [P, 2, Q, HEADS]), sb("val", [P, 2, Q, C]), sb("m", [P, 2, Q, C])
        with nc.Block() as block:
            @block.sync
            def _(sp):
                with sp.Fori(0, PAIRS) as i:
                    for u in range(2):
                        sp.wait_ge(sm["weighed"], i * 2 + u + 1)
                        sp.dma_start(val[:, u, :, :], rows_of(values, i * 2 + u)).then_inc(sm[f"v{u}"], 16)

            @block.gpsimd
            def _(pool):
                with pool.Fori(0, PAIRS) as i:
                    for u in range(2):
                        g = i * 2 + u
                        pool.wait_ge(sm["weighed"], g + 1)
                        pool.sem_inc(sm["pass_pool"], 1)
                        nc.gpsimd.tensor_copy(rows[:, u, :], k.pos_i[:, ds(g * Q, Q)]).then_inc(sm["rows"], 1)
                        pool.wait_ge(sm["rows"], g + 1)
                        pool.sem_inc(sm["pass_pool"], 1)
                        for q in range(Q):
                            pool.indirect_dma_start(w[:, u, q, :], None, weights[:, :], bass.IndirectOffsetOnAxis(
                                ap=rows[:, u, q:q + 1], axis=0)).then_inc(sm[f"w{u}"], 16)

            @block.vector
            def _(dve):
                dve.sem_inc(sm["weighed"], AHEAD)
                with dve.Fori(0, PAIRS) as i:
                    for u in range(2):
                        dve.wait_ge(sm[f"w{u}"], i * (16 * Q) + 16 * Q)
                        dve.wait_ge(sm[f"v{u}"], i * 16 + 16)
                        dve.wait_ge(sm[f"written{u}"], i * 16 + 16)
                        nc.vector.tensor_tensor(m[:, u, :, :].rearrange("p q (h d) -> p (q h) d", h=HEADS),
                                                val[:, u, :, :].rearrange("p q (h d) -> p (q h) d", h=HEADS),
                                                w[:, u, :, :].rearrange("p q h -> p (q h)").unsqueeze(2).to_broadcast([P, Q * HEADS, DH]),
                                                ALU.mult).then_inc(sm["weighed"], 1)

            @block.scalar
            def _(act):
                act.sem_inc(sm["written0"], 16)
                act.sem_inc(sm["written1"], 16)
                with act.Fori(0, PAIRS) as i:
                    for u in range(2):
                        act.wait_ge(sm["weighed"], i * 2 + u + 3)
                        act.dma_start(rows_of(messages, i * 2 + u), m[:, u, :, :]).then_inc(sm[f"written{u}"], 16)
                for u in range(2):
                    act.wait_ge(sm[f"written{u}"], 16 + 16 * PAIRS)
        end_phase(nc, sm)


def allocate(nc, ctx):
    k = Core()

    def sb(name, shape, dt=F32):
        return ctx.enter_context(nc.sbuf_tensor(name, shape, dt))

    k.dst_i = sb("dst_i", [P, ET], I32)
    k.src_i = sb("src_i", [P, ET], I32)
    k.dst_row = sb("dst_row", [P, ET], I32)
    k.pos_i = sb("pos_i", [P, ET], I32)
    k.ew = sb("ew", [P, ET])
    k.iota = sb("iota", [P, STEPS])
    k.pid = sb("pid", [P, 1])
    k.ident = sb("ident", [P, P])
    k.ones = sb("ones", [P, P])
    k.inv_deg = sb("inv_deg", [P, NT])
    k.inv_root = sb("inv_root", [P, NT])
    k.last_step = sb("last_step", [P, NT])
    k.last_step_i = sb("last_step_i", [1, NT], I32)
    k.left_step_i = sb("left_step_i", [1, ET], I32)
    k.keep = sb("keep", [P, STEPS])
    k.rel = sb("rel", [P, STEPS])
    k.slot_i = sb("slot_i", [1, STEPS], I32)
    k.arrive_i = sb("arrive_i", [1, STEPS], I32)
    k.partial = nc.dram_tensor("partial", [STEPS * P, C], F32).ap()
    return k


def kernel(**inputs):
    import numpy as np
    import concourse.bacc as bacc
    from concourse.bass_utils import run_bass_kernel_spmd

    def rows(a, fill, n=NP):
        a = np.asarray(a)
        return np.concatenate([a, np.full((n - a.shape[0],) + a.shape[1:], fill, a.dtype)])

    def by_tile(a, fill):
        a = rows(a, fill, ET * P)
        return np.ascontiguousarray(np.moveaxis(a.reshape((ET, P) + a.shape[1:]), 1, 0))

    arrays = {"x": rows(inputs["x"], 0)}
    arrays["src"] = by_tile(inputs["src"], PAD_SRC)
    arrays["src_rows"] = rows(inputs["src"], PAD_SRC)[None, :]
    arrays["dst"] = by_tile(inputs["dst"], PAD_DST)
    arrays["edge_weight"] = by_tile(inputs["edge_weight"], 0)
    arrays["no_source"] = np.full((1, ROW), -1, np.float32)
    arrays["mask"] = by_tile(inputs["edge_attr_8"], 0).reshape(P, ET * HEADS)
    for name in sorted(inputs):
        if name[0] == "L":
            a = np.asarray(inputs[name])
            if name in ("L3_gnn_Wq", "L3_gnn_Wk", "L3_gnn_Wv", "L3_gnn_Wo"):
                a = np.ascontiguousarray(a.T)
            arrays[name] = a[None, :] if a.ndim == 1 else a
    nc = bacc.Bacc("TRN2", target_bir_lowering=False, num_devices=1)
    ins = {n: nc.dram_tensor(f"in_{n}", a.shape, mybir.dt.from_np(a.dtype), kind="ExternalInput").ap() for n, a in arrays.items()}
    out = nc.dram_tensor("out_0", (NP, C), F32, kind="ExternalOutput").ap()
    program(nc, ins, out)
    r = run_bass_kernel_spmd(nc, [{f"in_{n}": a for n, a in arrays.items()}], core_ids=[0])
    return r.results[0]["out_0"][:N]


def program(nc, ins, out):
    def table(name, width=C):
        return nc.dram_tensor(name, [NP, width], F32).ap()

    with ExitStack() as ctx:
        k = allocate(nc, ctx)
        k.no_source = ins["no_source"]
        messages, x1, h1, x2, y2, y3, x3 = [table(n) for n in ("messages", "x1", "h1", "x2", "y2", "y3", "x3")]
        qv, keys, values = table("qv", 2 * C), table("keys"), table("values")
        by_source, weights = table("by_source", ROW), table("weights", HEADS)
        setup(nc, k, ins)
        count_and_rank(nc, k, ins)
        edge_mlp(nc, k, ins, messages)
        aggregate(nc, k, "agg0", messages, None)
        node_phase(nc, k, "l0", x1, "sum", residual=ins["x"])
        aggregate(nc, k, "agg1", x1, k.src_i)
        node_phase(nc, k, "l1a", h1, "mean", self_rows=x1, weights=(ins["L1_gnn_W_neigh1"], ins["L1_gnn_W_self1"]), bias=ins["L1_gnn_b1"], finish="relu")
        aggregate(nc, k, "agg2", h1, k.src_i)
        node_phase(nc, k, "l1b", x2, "mean", self_rows=h1, residual=x1, weights=(ins["L1_gnn_W_neigh2"], ins["L1_gnn_W_self2"]), bias=ins["L1_gnn_b2"], scaled_out=y2)
        aggregate(nc, k, "agg3", y2, k.src_i)
        node_phase(nc, k, "l2a", y3, "gcn", self_rows=y2, weights=(ins["L2_gnn_W1"],), bias=ins["L2_gnn_b1"], finish="relu", scaled_out=True)
        aggregate(nc, k, "agg4", y3, k.src_i)
        node_phase(nc, k, "l2b", x3, "gcn", self_rows=y3, residual=x2, weights=(ins["L2_gnn_W2"],), bias=ins["L2_gnn_b2"])
        project(nc, k, ins, x3, qv, keys)
        edge_scores(nc, k, ins, qv, keys, values, by_source)
        softmax_by_source(nc, k, by_source, weights)
        weigh(nc, k, values, weights, messages)
        aggregate(nc, k, "agg5", messages, None)
        node_phase(nc, k, "l3", out, "plain", residual=x3, weights=(ins["L3_gnn_Wo"],), bias=ins["L3_gnn_bo"])
```
